# Optimizing a Trainium2 kernel written in Bass

```python
import numpy as np
import jax
import jax.numpy as jnp

def _softmax(x, axis=-1):
    return jax.nn.softmax(x, axis=axis)

def _gelu(x):
    return jax.nn.gelu(x, approximate=True)

def _silu(x):
    return jax.nn.silu(x)

def _sigmoid(x):
    return jax.nn.sigmoid(x)

def _layernorm(x, axis=-1, eps=1e-05):
    m = jnp.mean(x, axis=axis, keepdims=True)
    v = jnp.var(x, axis=axis, keepdims=True)
    return (x - m) / jnp.sqrt(v + eps)

def _scatter_add(tgt, idx, src, axis=0):
    return tgt.at[idx].add(src)

def _segment_sum(src, seg, n):
    return jax.ops.segment_sum(src, seg, n)
kernel_name = 'mk_conv_seq_d2_conv_nchw64_r4_80fe60'

def setup_inputs(seed: int=0):
    np.random.seed(seed)
    _w = jnp.asarray

    def _rec_inputs():
        import jax
        import jax.numpy as jnp
        _gk = jax.random.key(seed)
        x = 1.508e-05 + 1 * jax.random.normal(jax.random.fold_in(_gk, 1), (16, 16, 64, 64), jnp.float32)
        return x
    x = _rec_inputs()

    def _L0_conv_setup():
        import jax, jax.numpy as jnp
        import numpy as np
        from jax import lax
        D = 2
        SIGMA = 2.0
        K = 9
        CH = 16
        PAD = (K - 1) // 2
        STRIDE = 1

        def make_gaussian_filter(sigma, k, channels):
            mean = (k - 1) / 2.0
            c = jnp.arange(k, dtype=jnp.float32) - mean
            g1 = jnp.exp(-c ** 2 / (2.0 * sigma ** 2))
            f = g1[:, None] * g1[None, :]
            f = f / jnp.sum(f)
            return jnp.broadcast_to(f[None, None], (channels, 1, k, k))

        def _blur(x, filt, groups):
            return lax.conv_general_dilated(x, filt, window_strides=(STRIDE, STRIDE), padding=[(PAD, PAD), (PAD, PAD)], dimension_numbers=('NCHW', 'OIHW', 'NCHW'), feature_group_count=groups)
        key = jax.random.key(seed)
        x = jax.random.normal(key, (16, CH, 64, 64), dtype=jnp.float32)
        filt = make_gaussian_filter(SIGMA, K, CH)
        return {'x': x, 'filt': filt}
    _L0_conv_all = _L0_conv_setup()
    _L0_conv_in = {k: v for k, v in _L0_conv_all.items() if k in ('filt',)}
    del _L0_conv_all

    def _L1_conv_setup():
        import jax, jax.numpy as jnp
        import numpy as np
        OUT_CHN, IN_CHN, K = (16, 16, 3)
        STRIDE, PADDING = (1, 1)

        def binary_activation(x):
            out_forward = jnp.sign(x)
            m1 = (x < -1).astype(jnp.float32)
            m2 = (x < 0).astype(jnp.float32)
            m3 = (x < 1).astype(jnp.float32)
            out1 = -1.0 * m1 + (x * x + 2.0 * x) * (1.0 - m1)
            out2 = out1 * m2 + (-x * x + 2.0 * x) * (1.0 - m2)
            out3 = out2 * m3 + 1.0 * (1.0 - m3)
            return jax.lax.stop_gradient(out_forward) - jax.lax.stop_gradient(out3) + out3

        def binarize_weights(weights):
            w = weights.reshape(OUT_CHN, IN_CHN, K, K)
            scale = jnp.mean(jnp.abs(w), axis=(1, 2, 3), keepdims=True)
            scale = jax.lax.stop_gradient(scale)
            bw_no_grad = scale * jnp.sign(w)
            clipped = jnp.clip(w, -1.0, 1.0)
            return jax.lax.stop_gradient(bw_no_grad) - jax.lax.stop_gradient(clipped) + clipped
        key = jax.random.key(seed)
        kx, kw = jax.random.split(key)
        x = jax.random.normal(kx, (16, 16, 56, 56), dtype=jnp.float32)
        weights = jax.random.uniform(kw, (OUT_CHN * IN_CHN * K * K, 1), dtype=jnp.float32) * 0.001
        return {'x': x, 'weights': weights}
    _L1_conv_all = _L1_conv_setup()
    _L1_conv_in = {k: v for k, v in _L1_conv_all.items() if k in ('weights',)}
    del _L1_conv_all
    return {'x': x, 'L0_conv_filt': _L0_conv_in['filt'], 'L1_conv_weights': _L1_conv_in['weights']}

def reference(x, L0_conv_filt, L1_conv_weights):
    import jax
    import jax.numpy as jnp

    def _L0_conv_ref(x, filt):
        import jax, jax.numpy as jnp
        import numpy as np
        from jax import lax
        D = 2
        SIGMA = 2.0
        K = 9
        CH = 16
        PAD = (K - 1) // 2
        STRIDE = 1

        def make_gaussian_filter(sigma, k, channels):
            mean = (k - 1) / 2.0
            c = jnp.arange(k, dtype=jnp.float32) - mean
            g1 = jnp.exp(-c ** 2 / (2.0 * sigma ** 2))
            f = g1[:, None] * g1[None, :]
            f = f / jnp.sum(f)
            return jnp.broadcast_to(f[None, None], (channels, 1, k, k))

        def _blur(x, filt, groups):
            return lax.conv_general_dilated(x, filt, window_strides=(STRIDE, STRIDE), padding=[(PAD, PAD), (PAD, PAD)], dimension_numbers=('NCHW', 'OIHW', 'NCHW'), feature_group_count=groups)
        y = _blur(x, filt, CH)
        ones = jnp.ones((1, 1) + x.shape[2:], dtype=x.dtype)
        w = _blur(ones, filt[:1], 1)
        return y / w

    def _L1_conv_ref(x, weights):
        import jax, jax.numpy as jnp
        import numpy as np
        OUT_CHN, IN_CHN, K = (16, 16, 3)
        STRIDE, PADDING = (1, 1)

        def binary_activation(x):
            out_forward = jnp.sign(x)
            m1 = (x < -1).astype(jnp.float32)
            m2 = (x < 0).astype(jnp.float32)
            m3 = (x < 1).astype(jnp.float32)
            out1 = -1.0 * m1 + (x * x + 2.0 * x) * (1.0 - m1)
            out2 = out1 * m2 + (-x * x + 2.0 * x) * (1.0 - m2)
            out3 = out2 * m3 + 1.0 * (1.0 - m3)
            return jax.lax.stop_gradient(out_forward) - jax.lax.stop_gradient(out3) + out3

        def binarize_weights(weights):
            w = weights.reshape(OUT_CHN, IN_CHN, K, K)
            scale = jnp.mean(jnp.abs(w), axis=(1, 2, 3), keepdims=True)
            scale = jax.lax.stop_gradient(scale)
            bw_no_grad = scale * jnp.sign(w)
            clipped = jnp.clip(w, -1.0, 1.0)
            return jax.lax.stop_gradient(bw_no_grad) - jax.lax.stop_gradient(clipped) + clipped
        bw = binarize_weights(weights)
        xa = binary_activation(x)
        y = jax.lax.conv_general_dilated(xa, bw, window_strides=(STRIDE, STRIDE), padding=[(PADDING, PADDING), (PADDING, PADDING)], dimension_numbers=('NCHW', 'OIHW', 'NCHW'))
        return y

    def _gn(v, G=32, eps=1e-05):
        B_, C_, H_, W_ = v.shape
        g = v.reshape(B_, G, C_ // G, H_, W_)
        m = jnp.mean(g, axis=(2, 3, 4), keepdims=True)
        s = jnp.var(g, axis=(2, 3, 4), keepdims=True)
        return ((g - m) / jnp.sqrt(s + eps)).reshape(v.shape)

    def _ln_c(v, eps=1e-06):
        m = jnp.mean(v, axis=1, keepdims=True)
        s = jnp.var(v, axis=1, keepdims=True)
        return (v - m) / jnp.sqrt(s + eps)

    def _ln_t(v, eps=1e-05):
        m = jnp.mean(v, axis=-1, keepdims=True)
        s = jnp.var(v, axis=-1, keepdims=True)
        return (v - m) / jnp.sqrt(s + eps)

    def _to_tokens(v):
        B_, C_, H_, W_ = v.shape
        return v.reshape(B_, C_, H_ * W_).transpose(0, 2, 1)

    def _from_tokens(t, like):
        B_, C_, H_, W_ = like.shape
        return t.transpose(0, 2, 1).reshape(B_, C_, H_, W_)
    x = _L0_conv_ref(x, L0_conv_filt)
    x = _L1_conv_ref(x, L1_conv_weights)
    return x

_drawn_inputs = setup_inputs


def setup_inputs(seed=0):
    import zlib

    import numpy as np

    out = dict(_drawn_inputs(seed))
    spreads = {}
    factors = {}
    for name, (base, spread) in spreads.items():
        noise = np.random.default_rng([zlib.crc32(name.encode()), seed]).standard_normal(out[name].shape)
        drawn = base * np.exp(spread * noise) if base else spread * noise
        out[name] = jnp.asarray(drawn.astype(out[name].dtype))
    for name, factor in factors.items():
        out[name] = (out[name] * factor).astype(out[name].dtype)
    return out
```

```python
import concourse.bass as bass
from concourse import mybir
from contextlib import ExitStack


def blur_binary_conv(nc, x, filt, weights, out):
    f32, f32r, bf16 = mybir.dt.float32, mybir.dt.float32r, mybir.dt.bfloat16
    ALU, ACT, AX = mybir.AluOpType, mybir.ActivationFunctionType, mybir.AxisListType

    B, C, H, W = x.shape
    K1 = filt.shape[2]
    K2 = 3
    CO = out.shape[1]
    WP = W // 2
    U = 2
    BU = B // U
    N = WP * B
    PAIRS = [0, -2, -1, 1, 2]
    SLOTS = K1 + 1
    PITCH = H - 1 - K1 // 2 + K1
    TAP0 = H - 1 - K1 // 2
    assert PITCH == TAP0 + K1

    KR, OR = 8, 6
    BLOCKS = -(-H // OR)
    LAST = H - OR * (BLOCKS - 1)
    TOP, BOTTOM = 3, 1
    ROWS = TOP + H + BOTTOM
    VLEN = K2 * CO * KR + KR

    R = 4

    filt_pad = nc.dram_tensor("filt_pad", (PITCH * (C * SLOTS + 2),), f32)
    sign_pad = nc.dram_tensor("sign_pad", (C, VLEN), bf16)
    act = nc.dram_tensor("act_signs", (C, ROWS, 2 * N), bf16)

    ctx = ExitStack()
    with ctx:
        def sb(name, shape, dt):
            return ctx.enter_context(nc.sbuf_tensor(name, shape, dt))

        def sem(name):
            return ctx.enter_context(nc.semaphore(name))

        filt_sb = sb("filt_sb", [C, K1 * K1], f32)
        filt_rows = sb("filt_rows", [C, SLOTS * PITCH], f32)
        w_in = sb("w_in", [C, CO, K2 * K2], f32)
        w_blk = sb("w_blk", [OR * CO, C * K2 * K2], f32)
        w_low = sb("w_low", [CO * LAST, C * K2 * K2], f32)
        w_abs = sb("w_abs", [CO * OR, C * K2 * K2], f32)
        w_sum = sb("w_sum", [CO * OR, 2], f32)
        scale_blk = sb("scale_blk", [CO * OR, 1], f32)
        scale_low = sb("scale_low", [CO * LAST, 1], f32)
        sign_rows = sb("sign_rows", [C, VLEN], bf16)
        zeros = sb("zeros", [C, TOP * N], f32)
        ones = sb("ones", [128, 2 * WP], f32r)
        inv_norm = sb("inv_norm", [128, WP, 2], f32)
        x_raw = sb("x_raw", [128, R, BU, W], f32)
        x_pair = sb("x_pair", [128, R, WP, B], f32)
        x_hi = sb("x_hi", [128, R, N], f32r)
        x_lo = sb("x_lo", [128, R, N], f32r)
        band = sb("band", [128, R, SLOTS, PITCH], f32)
        band_hi = sb("band_hi", [128, R, SLOTS, H], f32r)
        band_lo = sb("band_lo", [128, R, SLOTS, H], f32r)
        blur = sb("blur", [128, R, WP, B], f32)
        signs = sb("signs", [128, R, N], bf16)
        taps = sb("taps", [128, BLOCKS, 2, N], bf16)
        sign_band_in = sb("sign_band_in", [128, K2, CO, KR], bf16)
        sign_band = sb("sign_band", [128, K2, OR, CO], bf16)
        y_sb = sb("y_sb", [CO * OR, BLOCKS, B, W], f32)

        ps_blur = [ctx.enter_context(nc.psum_tensor(f"ps_blur{i}", [128, N], f32)) for i in range(R)]
        ps_y = [ctx.enter_context(nc.psum_tensor(f"ps_y{i}", [128, N], f32)) for i in range(4)]

        filt_loaded, w_loaded = sem("filt_loaded"), sem("w_loaded")
        rows_zeroed, signs_zeroed, zeros_ready, ones_ready = (
            sem("rows_zeroed"), sem("signs_zeroed"), sem("zeros_ready"), sem("ones_ready"))
        filt_placed, filt_padded = sem("filt_placed"), sem("filt_padded")
        sign_placed, sign_padded, sign_band_loaded = (
            sem("sign_placed"), sem("sign_padded"), sem("sign_band_loaded"))
        sign_band_ready, act_padded = sem("sign_band_ready"), sem("act_padded")
        x_loaded = [sem(f"x_loaded{i}") for i in range(R)]
        band_loaded = [sem(f"band_loaded{i}") for i in range(R)]
        x_paired, x_hi_ready, x_lo_ready = sem("x_paired"), sem("x_hi_ready"), sem("x_lo_ready")
        band_hi_ready, band_lo_ready = sem("band_hi_ready"), sem("band_lo_ready")
        norm_done, inv_ready = sem("norm_done"), sem("inv_ready")
        blur_done, blur_ready, signs_ready = sem("blur_done"), sem("blur_ready"), sem("signs_ready")
        signs_stored = [sem(f"signs_stored{i}") for i in range(R)]
        taps_loaded = sem("taps_loaded")
        abs_ready, sum_ready, scale_ready = sem("abs_ready"), sem("sum_ready"), sem("scale_ready")
        y_done = sem("y_done")
        even_ready, odd_ready = sem("even_ready"), sem("odd_ready")
        out_stored = sem("out_stored")

        block = ctx.enter_context(nc.Block())

        def landed(base, k, per_round):
            return base * (per_round // R) + per_round * (k // R + 1)

        @block.gpsimd
        def _(pool):
            nc.gpsimd.memset(filt_rows[:, :], 0.0).then_inc(rows_zeroed, 1)
            nc.gpsimd.memset(zeros[:, :], 0.0).then_inc(zeros_ready, 1)
            nc.gpsimd.memset(sign_rows[:, :], 0.0).then_inc(signs_zeroed, 1)
            nc.gpsimd.memset(ones[:, :].bitcast(f32), 1.0).then_inc(ones_ready, 1)

        @block.sync
        def _(sp):
            def load_x(c):
                for u in range(U):
                    sp.dma_start(x_raw[u * H:(u + 1) * H, c % R],
                                 x[u * BU:(u + 1) * BU, c].rearrange("i h w -> h i w")
                                 ).then_inc(x_loaded[c % R], 16)

            def load_band(c):
                for p in range(2):
                    sp.dma_start(band[p * H:(p + 1) * H, c % R].rearrange("r s m -> r (s m)"),
                                 bass.AP(filt_pad, (c * SLOTS + p) * PITCH, [[1, H], [1, SLOTS * PITCH]])
                                 ).then_inc(band_loaded[c % R], 16)

            sp.dma_start(filt_sb[:, :], filt.rearrange("c a h w -> c (a h w)")).then_inc(filt_loaded, 16)
            for k in range(2):
                load_x(k)
            sp.wait_ge(zeros_ready, 1)
            sp.dma_start(bass.AP(filt_pad, C * SLOTS * PITCH, [[1, 1], [1, 2 * PITCH]]),
                         zeros[0:1, 0:2 * PITCH]).then_inc(filt_padded, 16)
            sp.wait_ge(filt_placed, 1)
            sp.dma_start(bass.AP(filt_pad, 0, [[SLOTS * PITCH, C], [1, SLOTS * PITCH]]),
                         filt_rows[:, :]).then_inc(filt_padded, 16)
            sp.dma_start(w_in[:, :, :],
                         bass.AP(weights.tensor, 0, [[K2 * K2, C], [C * K2 * K2, CO], [1, K2 * K2]])
                         ).then_inc(w_loaded, 16)
            for dst, rows in ((w_blk, OR), (w_low, LAST)):
                sp.dma_start(dst[:, :], bass.AP(weights.tensor, 0,
                                                [[0, rows], [C * K2 * K2, CO], [1, C * K2 * K2]])
                             ).then_inc(w_loaded, 16)
            sp.wait_ge(filt_padded, 32)
            load_band(0)
            load_band(1)
            for k in range(2, R):
                load_x(k)
                load_band(k)
            sp.dma_start(act[:, 0:TOP, :].rearrange("c r n -> c (r n)"),
                         zeros[:, :].bitcast(bf16)).then_inc(act_padded, 16)
            sp.dma_start(act[:, TOP + H, :], zeros[:, 0:N].bitcast(bf16)).then_inc(act_padded, 16)
            sp.wait_ge(sign_placed, K2)
            sp.dma_start(sign_pad[:, :], sign_rows[:, :]).then_inc(sign_padded, 16)
            for c in range(R, C):
                sp.wait_ge(x_paired, c - R + 1)
                load_x(c)
                sp.wait_ge(band_lo_ready, c - R + 1)
                load_band(c)
            sp.wait_ge(sign_padded, 16)
            for c in range(C):
                sp.dma_start(sign_band_in[c * KR:(c + 1) * KR].rearrange("r d o m -> r (d o m)"),
                             bass.AP(sign_pad, c * VLEN, [[1, KR], [1, K2 * CO * KR]])
                             ).then_inc(sign_band_loaded, 16)
            sp.wait_ge(act_padded, 32)
            for c in range(C):
                sp.wait_ge(signs_stored[c % R], landed(0, c, 32))
                sp.dma_start(taps[c * KR:(c + 1) * KR].rearrange("r b p n -> r b (p n)"),
                             bass.AP(act, c * ROWS * 2 * N,
                                     [[2 * N, KR], [OR * 2 * N, BLOCKS], [1, 2 * N]])
                             ).then_inc(taps_loaded, 16)

            for n in range(BLOCKS):
                rows = OR if n else LAST
                sp.wait_ge(even_ready, n + 1)
                sp.wait_ge(odd_ready, n + 1)
                for r in range(rows):
                    sp.dma_start(out[:, :, OR * (BLOCKS - 1 - n) + r, :].rearrange("i c w -> c i w"),
                                 y_sb[r * CO:(r + 1) * CO, n]).then_inc(out_stored, 16)
            sp.wait_ge(out_stored, 16 * H)

        @block.vector
        def _(dve):
            dve.wait_ge(rows_zeroed, 1)
            dve.wait_ge(filt_loaded, 16)
            nc.vector.tensor_copy(
                filt_rows[:, :].rearrange("c (s m) -> c s m", m=PITCH)[:, 1:1 + K1, TAP0:TAP0 + K1],
                filt_sb[:, :].rearrange("c (y x) -> c x y", x=K1)).then_inc(filt_placed, 1)

            def pair_columns(base, k):
                dve.wait_ge(x_loaded[k % R], landed(base, k, 32))
                for u in range(U):
                    for p in range(2):
                        last = nc.vector.tensor_copy(
                            x_pair[p * H:(p + 1) * H, k % R, :, u * BU:(u + 1) * BU],
                            x_raw[u * H:(u + 1) * H, k % R, :, p::2].rearrange("h i j -> h j i"))
                last.then_inc(x_paired, 1)

            def low_parts(base, k):
                dve.wait_ge(band_hi_ready, base + k + 1)
                if not (isinstance(base, int) and base + k < R):
                    dve.wait_ge(blur_done, base + k - R + 1)
                nc.vector.tensor_tensor(band_lo[:, k % R], band[:, k % R, :, 0:H],
                                        band_hi[:, k % R].bitcast(f32), ALU.subtract
                                        ).then_inc(band_lo_ready, 1)
                dve.wait_ge(x_hi_ready, base + k + 1)
                nc.vector.tensor_tensor(x_lo[:, k % R], x_pair[:, k % R].rearrange("q j i -> q (j i)"),
                                        x_hi[:, k % R].bitcast(f32), ALU.subtract
                                        ).then_inc(x_lo_ready, 1)

            def normalise(base, k):
                dve.wait_ge(blur_done, base + k + 1)
                if not (isinstance(base, int) and base + k < R):
                    dve.wait_ge(signs_ready, base + k - R + 1)
                nc.vector.tensor_tensor(
                    blur[:, k % R], ps_blur[k % R][:, :].rearrange("q (j i) -> q j i", i=B),
                    inv_norm[:, :, 0:1].to_broadcast([128, WP, B]), ALU.mult).then_inc(blur_ready, 1)

            def inverse_norm():
                dve.wait_ge(norm_done, 1)
                nc.vector.reciprocal(inv_norm[:, :, :],
                                     ps_y[0][:, 0:2 * WP].rearrange("q (j i) -> q j i", i=2)
                                     ).then_inc(inv_ready, 1)
                dve.wait_ge(inv_ready, 1)

            def weight_scales():
                dve.wait_ge(w_loaded, 48)
                n = C * K2 * K2
                for i, (w, s) in enumerate(((w_blk, scale_blk), (w_low, scale_low))):
                    q = w.shape[0]
                    nc.vector.scalar_tensor_tensor(out=w_abs[0:q, :], in0=w[:, :], scalar=-1.0, in1=w[:, :],
                                                   op0=ALU.mult, op1=ALU.max).then_inc(abs_ready, 1)
                    dve.wait_ge(abs_ready, i + 1)
                    nc.vector.reduce_sum(w_sum[0:q, i:i + 1], w_abs[0:q, :], axis=AX.X
                                         ).then_inc(sum_ready, 1)
                    dve.wait_ge(sum_ready, i + 1)
                    nc.vector.tensor_scalar(s[:, :], w_sum[0:q, i:i + 1], 1.0 / n, None, ALU.mult
                                            ).then_inc(scale_ready, 1)

            def step(base, k):
                first = isinstance(base, int)
                if not first or base + k < C:
                    pair_columns(base, k)
                if not first or 0 <= base + k - 1 < C:
                    low_parts(base, k - 1)
                if not first or base + k - 3 >= 0:
                    normalise(base, k - 3)

            for k in range(2 * R):
                if k == 3:
                    inverse_norm()
                step(0, k)
            with dve.Fori(2 * R, C - R + 1, R) as c0:
                for k in range(R):
                    step(c0, k)
            for k in range(3):
                step(C, k)
            weight_scales()

            dve.wait_ge(sign_band_loaded, 16 * C)
            nc.vector.tensor_copy(sign_band[:, :, :, :].rearrange("q d m o -> q d o m"),
                                  sign_band_in[:, :, :, 0:OR]).then_inc(sign_band_ready, 1)
            dve.wait_ge(scale_ready, 2)

            def scale_odd(n, slot, rows, s):
                dve.wait_ge(y_done, n * 2 + 2)
                q = CO * rows
                nc.vector.tensor_scalar(
                    y_sb[0:q, bass.ds(n, 1), :, 1::2].rearrange("q a i j -> q j (a i)"),
                    ps_y[2 * slot + 1][0:q, :].rearrange("q (j i) -> q j i", i=B),
                    s[:, 0:1], None, ALU.mult).then_inc(odd_ready, 1)

            scale_odd(0, 0, LAST, scale_low)
            with dve.Fori(1, BLOCKS - 1, 2) as n:
                scale_odd(n, 1, OR, scale_blk)
                scale_odd(n + 1, 0, OR, scale_blk)

        @block.scalar
        def _(act_e):
            def high_parts(base, k):
                if not (isinstance(base, int) and base + k < R):
                    act_e.wait_ge(blur_done, base + k - R + 1)
                act_e.wait_ge(band_loaded[k % R], landed(base, k, 32))
                nc.scalar.activation(band_hi[:, k % R], band[:, k % R, :, 0:H], ACT.Copy
                                     ).then_inc(band_hi_ready, 1)
                act_e.wait_ge(x_paired, base + k + 1)
                nc.scalar.activation(x_hi[:, k % R], x_pair[:, k % R].rearrange("q j i -> q (j i)"),
                                     ACT.Copy).then_inc(x_hi_ready, 1)

            def take_signs(base, k):
                act_e.wait_ge(blur_ready, base + k + 1)
                if not (isinstance(base, int) and base + k < R):
                    act_e.wait_ge(signs_stored[k % R], landed(base, k - R, 32))
                nc.scalar.activation(signs[:, k % R], blur[:, k % R].rearrange("q j i -> q (j i)"),
                                     ACT.Sign).then_inc(signs_ready, 1)
                act_e.wait_ge(signs_ready, base + k + 1)
                for p in range(2):
                    dst = act[bass.ds(base + k, 1), TOP:TOP + H, p * N:(p + 1) * N]
                    act_e.dma_start(dst.rearrange("c m n -> (c m) n"), signs[p * H:(p + 1) * H, k % R]
                                    ).then_inc(signs_stored[k % R], 16)

            def step(base, k):
                first = isinstance(base, int)
                if not first or base + k < C:
                    high_parts(base, k)
                if not first or base + k - 3 >= 0:
                    take_signs(base, k - 3)

            def place_signs():
                act_e.wait_ge(w_loaded, 48)
                act_e.wait_ge(signs_zeroed, 1)
                rows = sign_rows[:, 0:K2 * CO * KR].rearrange("c (d o m) -> c d o m", o=CO, m=KR)
                for dy in range(K2):
                    nc.scalar.activation(
                        rows[:, :, :, KR - 1 - dy],
                        w_in[:, :, dy * K2:(dy + 1) * K2].rearrange("c o d -> c d o"),
                        ACT.Sign).then_inc(sign_placed, 1)

            for k in range(2 * R):
                if k == 3:
                    place_signs()
                step(0, k)
            with act_e.Fori(2 * R, C - R + 1, R) as c0:
                for k in range(R):
                    step(c0, k)
            for k in range(3):
                step(C, k)

            def scale_even(n, slot, rows, s):
                act_e.wait_ge(y_done, n * 2 + 1)
                q = CO * rows
                nc.scalar.activation(
                    y_sb[0:q, bass.ds(n, 1), :, 0::2].rearrange("q a i j -> q j (a i)"),
                    ps_y[2 * slot][0:q, :].rearrange("q (j i) -> q j i", i=B),
                    ACT.Copy, scale=s[:, 0:1]).then_inc(even_ready, 1)

            act_e.wait_ge(scale_ready, 2)
            scale_even(0, 0, LAST, scale_low)
            with act_e.Fori(1, BLOCKS - 1, 2) as n:
                scale_even(n, 1, OR, scale_blk)
                scale_even(n + 1, 0, OR, scale_blk)

        @block.tensor
        def _(pe):
            def columns(k, per):
                lo, hi = max(0, -k), WP - max(0, k)
                return slice(lo * per, hi * per), slice((lo + k) * per, (hi + k) * per)

            def bands(tile, slot, k):
                s = 2 * (k + 2)
                return tile[:, slot, s:s + 2].rearrange("q s m -> q (s m)")

            pe.wait_ge(ones_ready, 1)
            pe.wait_ge(band_lo_ready, 1)
            for j, tile in enumerate((band_hi, band_lo)):
                for i, k in enumerate(PAIRS):
                    o, r = columns(k, 2)
                    last = nc.tensor.matmul(ps_y[0][:, o], bands(tile, 0, k), ones[:, r],
                                            start=(i + j == 0), stop=(i == 4 and j == 1))
            last.then_inc(norm_done, 1)

            def blur_channel(base, k):
                pe.wait_ge(band_lo_ready, base + k + 1)
                pe.wait_ge(x_lo_ready, base + k + 1)
                if not (isinstance(base, int) and base + k < R):
                    pe.wait_ge(blur_ready, base + k - R + 1)
                slot = k % R
                parts = ((band_hi, x_hi), (band_hi, x_lo), (band_lo, x_hi))
                for j, (b, v) in enumerate(parts):
                    for i, off in enumerate(PAIRS):
                        o, r = columns(off, B)
                        last = nc.tensor.matmul(ps_blur[slot][:, o], bands(b, slot, off), v[:, slot, r],
                                                start=(i + j == 0), stop=(i == 4 and j == 2))
                last.then_inc(blur_done, 1)

            for k in range(R):
                blur_channel(0, k)
            with pe.Fori(R, C - R + 1, R) as c0:
                for k in range(R):
                    blur_channel(c0, k)

            pe.wait_ge(inv_ready, 1)
            pe.wait_ge(sign_band_ready, 1)
            pe.wait_ge(taps_loaded, 16 * C)

            def binary_conv(n, slot, rows, reused):
                plan = {0: ((1, 1, 0), (2, 0, 0), (0, 0, -1)), 1: ((1, 0, 0), (0, 1, 0), (2, 1, 1))}
                for q in range(2):
                    if reused:
                        pe.wait_ge((even_ready, odd_ready)[q], n - 1)
                    for i, (dx, place, off) in enumerate(plan[q]):
                        o, r = columns(off, B)
                        last = nc.tensor.matmul(
                            ps_y[2 * slot + q][0:CO * rows, o],
                            sign_band[:, dx, 0:rows].rearrange("q m o -> q (m o)"),
                            taps[:, bass.ds(n, 1), place, r].rearrange("q a n -> q (a n)"),
                            start=(i == 0), stop=(i == 2))
                    last.then_inc(y_done, 1)

            binary_conv(0, 0, LAST, False)
            binary_conv(1, 1, OR, False)
            binary_conv(2, 0, OR, True)
            with pe.Fori(3, BLOCKS - 1, 2) as n:
                binary_conv(n, 1, OR, True)
                binary_conv(n + 1, 0, OR, True)


_INS = ["x", "L0_conv_filt", "L1_conv_weights"]


def kernel(**inputs):
    import numpy as _np
    import concourse.bacc as _bacc
    from concourse import mybir as _mybir
    from concourse.bass_utils import run_bass_kernel_spmd as _run

    nc = _bacc.Bacc("TRN2", target_bir_lowering=False, num_devices=1)
    arrays, args = {}, []
    for name in _INS:
        a = _np.ascontiguousarray(inputs[name])
        arrays[f"in_{name}_dram"] = a
        args.append(nc.dram_tensor(f"in_{name}_dram", a.shape, _mybir.dt.from_np(a.dtype), kind="ExternalInput").ap())
    dt = _mybir.dt.from_np(_np.dtype("float32"))
    args.append(nc.dram_tensor("out_0_dram", inputs["x"].shape, dt, kind="ExternalOutput").ap())
    blur_binary_conv(nc, *args)
    r = _run(nc, [arrays], core_ids=[0])
    return r.results[0]["out_0_dram"]
```

```python
import concourse.bass as bass
from concourse import mybir
from contextlib import ExitStack


def blur_binary_conv(nc, x, filt, weights, out):
    f32, f32r, bf16 = mybir.dt.float32, mybir.dt.float32r, mybir.dt.bfloat16
    ALU, ACT, AX = mybir.AluOpType, mybir.ActivationFunctionType, mybir.AxisListType

    B, C, H, W = x.shape
    K1 = filt.shape[2]
    K2 = 3
    CO = out.shape[1]
    WP = W // 2
    PAIR = 2
    N = WP * B
    PAIRS = [0, -2, -1, 1, 2]
    SLOTS = K1 + 1
    PITCH = H - 1 - K1 // 2 + K1
    TAP0 = H - 1 - K1 // 2
    assert PITCH == TAP0 + K1

    KR, OR = 8, 6
    BLOCKS = -(-H // OR)
    LAST = H - OR * (BLOCKS - 1)
    RP = 2
    HALF = 64
    USED = OR // RP * CO
    TOP, BOTTOM = 3, 1
    ROWS = TOP + H + BOTTOM
    VLEN = K2 * CO * KR + KR

    R = 4

    filt_pad = nc.dram_tensor("filt_pad", (PITCH * (C * SLOTS + 2),), f32)
    sign_pad = nc.dram_tensor("sign_pad", (C, VLEN), bf16)
    act = nc.dram_tensor("act_signs", (C, ROWS, 2, N), bf16)

    ctx = ExitStack()
    with ctx:
        def sb(name, shape, dt):
            return ctx.enter_context(nc.sbuf_tensor(name, shape, dt))

        def sem(name):
            return ctx.enter_context(nc.semaphore(name))

        filt_sb = sb("filt_sb", [C, K1 * K1], f32)
        filt_rows = sb("filt_rows", [C, SLOTS * PITCH], f32)
        w_in = sb("w_in", [C, CO, K2 * K2], f32)
        w_out = sb("w_out", [128, C * K2 * K2], f32)
        w_abs = sb("w_abs", [128, C * K2 * K2], f32)
        w_sum = sb("w_sum", [128, 1], f32)
        scale = sb("scale", [128, 1], f32)
        sign_rows = sb("sign_rows", [C, VLEN], bf16)
        zeros = sb("zeros", [C, TOP * N], f32)
        ones = sb("ones", [128, 2 * WP], f32r)
        inv_norm = sb("inv_norm", [128, WP, 2], f32)
        x_raw = sb("x_raw", [128, R // PAIR, B, W], f32)
        x_pair = sb("x_pair", [128, R, WP, B], f32)
        x_hi = sb("x_hi", [128, R, N], f32r)
        x_lo = sb("x_lo", [128, R, N], f32r)
        band = sb("band", [128, R, SLOTS, PITCH], f32)
        band_hi = sb("band_hi", [128, R, SLOTS // 2, H, 2], f32r)
        band_lo = sb("band_lo", [128, R, SLOTS // 2, H, 2], f32r)
        blur = sb("blur", [128, R, WP, B], f32)
        signs = sb("signs", [128, R, N], bf16)
        taps = sb("taps", [128, BLOCKS, 2, N], bf16)
        sign_band_in = sb("sign_band_in", [128, K2, CO, KR], bf16)
        sign_band = sb("sign_band", [128, K2, RP, HALF], bf16)
        y_sb = sb("y_sb", [128, (BLOCKS + 1) // 2, B, RP, W], f32)

        ps_blur = [ctx.enter_context(nc.psum_tensor(f"ps_blur{i}", [128, N], f32)) for i in range(R)]
        ps_y = [ctx.enter_context(nc.psum_tensor(f"ps_y{i}", [128, N], f32)) for i in range(4)]

        filt_loaded, w_loaded = sem("filt_loaded"), sem("w_loaded")
        rows_zeroed, signs_zeroed, zeros_ready, ones_ready = (
            sem("rows_zeroed"), sem("signs_zeroed"), sem("zeros_ready"), sem("ones_ready"))
        filt_placed, filt_padded = sem("filt_placed"), sem("filt_padded")
        sign_placed, sign_padded, sign_band_loaded = (
            sem("sign_placed"), sem("sign_padded"), sem("sign_band_loaded"))
        sign_band_zeroed, sign_band_ready = sem("sign_band_zeroed"), sem("sign_band_ready")
        act_padded = sem("act_padded")
        x_loaded = [sem(f"x_loaded{i}") for i in range(R // PAIR)]
        band_loaded = [sem(f"band_loaded{i}") for i in range(R // PAIR)]
        x_paired, x_hi_ready, x_lo_ready = sem("x_paired"), sem("x_hi_ready"), sem("x_lo_ready")
        band_hi_ready, band_lo_ready = sem("band_hi_ready"), sem("band_lo_ready")
        norm_done, inv_ready = sem("norm_done"), sem("inv_ready")
        blur_done, blur_ready, signs_ready = sem("blur_done"), sem("blur_ready"), sem("signs_ready")
        signs_stored = [sem(f"signs_stored{i}") for i in range(R // PAIR)]
        taps_loaded = sem("taps_loaded")
        abs_ready, sum_ready, scale_ready = sem("abs_ready"), sem("sum_ready"), sem("scale_ready")
        y_done = sem("y_done")
        even_ready, odd_ready = sem("even_ready"), sem("odd_ready")
        out_stored = sem("out_stored")

        block = ctx.enter_context(nc.Block())

        def pair_slot(k):
            return k // PAIR % (R // PAIR)

        def landed(base, k, per_round):
            return base * (per_round // R) + per_round * (k // R + 1)

        def slots(k):
            return band[:, k % R, :, 0:H].rearrange("q (o s) m -> q o s m", s=2)

        def by_slot(tile, k):
            return tile[:, k % R].rearrange("q o m s -> q o s m")

        @block.gpsimd
        def _(pool):
            nc.gpsimd.memset(filt_rows[:, :], 0.0).then_inc(rows_zeroed, 1)
            nc.gpsimd.memset(zeros[:, :], 0.0).then_inc(zeros_ready, 1)
            nc.gpsimd.memset(ones[:, :].bitcast(f32), 1.0).then_inc(ones_ready, 1)
            nc.gpsimd.memset(sign_rows[:, :], 0.0).then_inc(signs_zeroed, 1)
            nc.gpsimd.memset(sign_band[:, :, :, :], 0.0).then_inc(sign_band_zeroed, 1)
            pool.dma_start(w_in[:, :, :],
                           bass.AP(weights.tensor, 0, [[K2 * K2, C], [C * K2 * K2, CO], [1, K2 * K2]])
                           ).then_inc(w_loaded, 16)
            pool.dma_start(w_out[:, :],
                           bass.AP(weights.tensor, 0, [[0, 128 // CO], [C * K2 * K2, CO], [1, C * K2 * K2]])
                           ).then_inc(w_loaded, 16)
            pool.wait_ge(zeros_ready, 1)
            pool.dma_start(act[:, 0:TOP].rearrange("c r p n -> c (r p n)"),
                           zeros[:, :].bitcast(bf16)).then_inc(act_padded, 16)
            pool.dma_start(act[:, TOP + H].rearrange("c p n -> c (p n)"),
                           zeros[:, 0:N].bitcast(bf16)).then_inc(act_padded, 16)
            pool.wait_ge(sign_placed, K2)
            pool.dma_start(sign_pad[:, :], sign_rows[:, :]).then_inc(sign_padded, 16)
            pool.wait_ge(sign_padded, 16)
            for kr in range(KR):
                pool.dma_start(sign_band_in[kr::KR].rearrange("c d o m -> c (d o m)"),
                               sign_pad[:, kr:kr + K2 * CO * KR]).then_inc(sign_band_loaded, 16)

        @block.sync
        def _(sp):
            def load_x(t):
                sp.dma_start(x_raw[:, t % (R // PAIR)],
                             x[:, PAIR * t:PAIR * (t + 1)].rearrange("i c h w -> (c h) i w")
                             ).then_inc(x_loaded[t % (R // PAIR)], 16)

            def load_band(t):
                s = t % (R // PAIR) * PAIR
                for p in range(2):
                    sp.dma_start(band[p * H:(p + 1) * H, s:s + PAIR].rearrange("r c s m -> r (c s m)"),
                                 bass.AP(filt_pad, (PAIR * t * SLOTS + p) * PITCH,
                                         [[1, H], [1, PAIR * SLOTS * PITCH]])
                                 ).then_inc(band_loaded[t % (R // PAIR)], 16)

            sp.dma_start(filt_sb[:, :], filt.rearrange("c a h w -> c (a h w)")).then_inc(filt_loaded, 16)
            sp.wait_ge(zeros_ready, 1)
            sp.dma_start(bass.AP(filt_pad, C * SLOTS * PITCH, [[1, 1], [1, 2 * PITCH]]),
                         zeros[0:1, 0:2 * PITCH]).then_inc(filt_padded, 16)
            load_x(0)
            sp.wait_ge(filt_placed, 1)
            sp.dma_start(bass.AP(filt_pad, 0, [[SLOTS * PITCH, C], [1, SLOTS * PITCH]]),
                         filt_rows[:, :]).then_inc(filt_padded, 16)
            sp.wait_ge(filt_padded, 32)
            load_band(0)
            load_x(1)
            load_band(1)
            for t in range(R // PAIR, C // PAIR):
                sp.wait_ge(x_paired, PAIR * (t + 1) - R)
                load_x(t)
                sp.wait_ge(band_lo_ready, PAIR * (t + 1) - R)
                load_band(t)
            sp.wait_ge(act_padded, 32)
            for c in range(C):
                if c % PAIR == 0:
                    sp.wait_ge(signs_stored[pair_slot(c)], landed(0, c, 16))
                sp.dma_start(taps[c * KR:(c + 1) * KR].rearrange("r b p n -> r b (p n)"),
                             bass.AP(act, c * ROWS * 2 * N,
                                     [[2 * N, KR], [OR * 2 * N, BLOCKS], [1, 2 * N]])
                             ).then_inc(taps_loaded, 16)
            for n in range(BLOCKS):
                sp.wait_ge(even_ready, n + 1)
                sp.wait_ge(odd_ready, n + 1)
                for r in range(0, OR if n else LAST, RP):
                    q = n % 2 * HALF + r // RP * CO
                    row = OR * (BLOCKS - 1 - n) + r
                    sp.dma_start(out[:, :, row:row + RP].rearrange("i c r w -> c i (r w)"),
                                 y_sb[q:q + CO, n // 2].rearrange("q i r w -> q i (r w)")
                                 ).then_inc(out_stored, 16)
            sp.wait_ge(out_stored, 16 * H // RP)

        @block.vector
        def _(dve):
            dve.wait_ge(rows_zeroed, 1)
            dve.wait_ge(filt_loaded, 16)
            nc.vector.tensor_copy(
                filt_rows[:, :].rearrange("c (s m) -> c s m", m=PITCH)[:, 1:1 + K1, TAP0:TAP0 + K1],
                filt_sb[:, :].rearrange("c (y x) -> c x y", x=K1)).then_inc(filt_placed, 1)

            def pair_columns(base, k):
                dve.wait_ge(x_loaded[pair_slot(k)], landed(base, k, 16))
                u = k % PAIR
                for p in range(2):
                    last = nc.vector.tensor_copy(
                        x_pair[p * H:(p + 1) * H, k % R],
                        x_raw[u * H:(u + 1) * H, pair_slot(k), :, p::2].rearrange("h i j -> h j i"))
                last.then_inc(x_paired, 1)

            def low_parts(base, k):
                dve.wait_ge(band_hi_ready, base + k + 1)
                if not (isinstance(base, int) and base + k < R):
                    dve.wait_ge(blur_done, base + k - R + 1)
                nc.vector.tensor_tensor(by_slot(band_lo, k), slots(k), by_slot(band_hi, k).bitcast(f32),
                                        ALU.subtract).then_inc(band_lo_ready, 1)
                dve.wait_ge(x_hi_ready, base + k + 1)
                nc.vector.tensor_tensor(x_lo[:, k % R], x_pair[:, k % R].rearrange("q j i -> q (j i)"),
                                        x_hi[:, k % R].bitcast(f32), ALU.subtract
                                        ).then_inc(x_lo_ready, 1)

            def normalise(base, k):
                dve.wait_ge(blur_done, base + k + 1)
                if not (isinstance(base, int) and base + k < R):
                    dve.wait_ge(signs_ready, base + k - R + 1)
                nc.vector.tensor_tensor(
                    blur[:, k % R], ps_blur[k % R][:, :].rearrange("q (j i) -> q j i", i=B),
                    inv_norm[:, :, 0:1].to_broadcast([128, WP, B]), ALU.mult).then_inc(blur_ready, 1)

            def inverse_norm():
                dve.wait_ge(norm_done, 1)
                nc.vector.reciprocal(inv_norm[:, :, :],
                                     ps_y[0][:, 0:2 * WP].rearrange("q (j i) -> q j i", i=2)
                                     ).then_inc(inv_ready, 1)
                dve.wait_ge(inv_ready, 1)

            def weight_scales():
                dve.wait_ge(w_loaded, 32)
                nc.vector.scalar_tensor_tensor(out=w_abs[:, :], in0=w_out[:, :], scalar=-1.0,
                                               in1=w_out[:, :], op0=ALU.mult, op1=ALU.max
                                               ).then_inc(abs_ready, 1)
                dve.wait_ge(abs_ready, 1)
                nc.vector.reduce_sum(w_sum[:, :], w_abs[:, :], axis=AX.X).then_inc(sum_ready, 1)
                dve.wait_ge(sum_ready, 1)
                nc.vector.tensor_scalar(scale[:, :], w_sum[:, :], 1.0 / (C * K2 * K2), None, ALU.mult
                                        ).then_inc(scale_ready, 1)

            def sign_matrices():
                dve.wait_ge(sign_band_zeroed, 1)
                dve.wait_ge(sign_band_loaded, 16 * KR)
                for rp in range(RP):
                    nc.vector.tensor_copy(
                        sign_band[:, :, rp, 0:USED].rearrange("q d (m o) -> q d o m", o=CO),
                        sign_band_in[:, :, :, rp:OR:RP]).then_inc(sign_band_ready, 1)

            def step(base, k):
                first = isinstance(base, int)
                if not first or base + k < C:
                    pair_columns(base, k)
                if not first or 0 <= base + k - 1 < C:
                    low_parts(base, k - 1)
                if not first or base + k - 3 >= 0:
                    normalise(base, k - 3)

            for k in range(2 * R):
                if k == 3:
                    inverse_norm()
                if k == 5:
                    weight_scales()
                if k == 7:
                    sign_matrices()
                step(0, k)
            with dve.Fori(2 * R, C - R + 1, R) as c0:
                for k in range(R):
                    step(c0, k)
            for k in range(3):
                step(C, k)

            def scale_odd(n, half, at):
                dve.wait_ge(y_done, n * 2 + 2)
                for rp in range(RP):
                    q = rp * HALF
                    last = nc.vector.tensor_scalar(
                        y_sb[half * HALF:half * HALF + USED, bass.ds(at, 1), :, rp, 1::2
                             ].rearrange("q a i j -> q j (a i)"),
                        ps_y[2 * half + 1][q:q + USED, :].rearrange("q (j i) -> q j i", i=B),
                        scale[q:q + USED, 0:1], None, ALU.mult)
                last.then_inc(odd_ready, 1)

            dve.wait_ge(scale_ready, 1)
            scale_odd(0, 0, 0)
            with dve.Fori(0, BLOCKS // 2, 1) as j:
                scale_odd(2 * j + 1, 1, j)
                scale_odd(2 * j + 2, 0, j + 1)

        @block.scalar
        def _(act_e):
            def high_parts(base, k):
                if not (isinstance(base, int) and base + k < R):
                    act_e.wait_ge(blur_done, base + k - R + 1)
                act_e.wait_ge(band_loaded[pair_slot(k)], landed(base, k, 32))
                nc.scalar.activation(by_slot(band_hi, k), slots(k), ACT.Copy).then_inc(band_hi_ready, 1)
                act_e.wait_ge(x_paired, base + k + 1)
                nc.scalar.activation(x_hi[:, k % R], x_pair[:, k % R].rearrange("q j i -> q (j i)"),
                                     ACT.Copy).then_inc(x_hi_ready, 1)

            def take_signs(base, k):
                act_e.wait_ge(blur_ready, base + k + 1)
                if not (isinstance(base, int) and base + k < R):
                    act_e.wait_ge(signs_stored[pair_slot(k)], landed(base, k - R, 16))
                nc.scalar.activation(signs[:, k % R], blur[:, k % R].rearrange("q j i -> q (j i)"),
                                     ACT.Sign).then_inc(signs_ready, 1)
                if k % PAIR == PAIR - 1:
                    act_e.wait_ge(signs_ready, base + k + 1)
                    s = pair_slot(k) * PAIR
                    act_e.dma_start(
                        act[bass.ds(base + (k - PAIR + 1), PAIR), TOP:TOP + H].rearrange(
                            "c m p n -> (m p) c n"),
                        signs[:, s:s + PAIR]).then_inc(signs_stored[pair_slot(k)], 16)

            def step(base, k):
                first = isinstance(base, int)
                if not first or base + k < C:
                    high_parts(base, k)
                if not first or base + k - 3 >= 0:
                    take_signs(base, k - 3)

            def place_signs():
                act_e.wait_ge(w_loaded, 32)
                act_e.wait_ge(signs_zeroed, 1)
                rows = sign_rows[:, 0:K2 * CO * KR].rearrange("c (d o m) -> c d o m", o=CO, m=KR)
                for dy in range(K2):
                    nc.scalar.activation(
                        rows[:, :, :, KR - 1 - dy],
                        w_in[:, :, dy * K2:(dy + 1) * K2].rearrange("c o d -> c d o"),
                        ACT.Sign).then_inc(sign_placed, 1)

            for k in range(2 * R):
                if k == 3:
                    place_signs()
                step(0, k)
            with act_e.Fori(2 * R, C - R + 1, R) as c0:
                for k in range(R):
                    step(c0, k)
            for k in range(3):
                step(C, k)

            def scale_even(n, half, at):
                act_e.wait_ge(y_done, n * 2 + 1)
                for rp in range(RP):
                    q = rp * HALF
                    last = nc.scalar.activation(
                        y_sb[half * HALF:half * HALF + USED, bass.ds(at, 1), :, rp, 0::2
                             ].rearrange("q a i j -> q j (a i)"),
                        ps_y[2 * half][q:q + USED, :].rearrange("q (j i) -> q j i", i=B),
                        ACT.Copy, scale=scale[q:q + USED, 0:1])
                last.then_inc(even_ready, 1)

            act_e.wait_ge(scale_ready, 1)
            scale_even(0, 0, 0)
            with act_e.Fori(0, BLOCKS // 2, 1) as j:
                scale_even(2 * j + 1, 1, j)
                scale_even(2 * j + 2, 0, j + 1)

        @block.tensor
        def _(pe):
            def columns(k, per):
                lo, hi = max(0, -k), WP - max(0, k)
                return slice(lo * per, hi * per), slice((lo + k) * per, (hi + k) * per)

            def bands(tile, slot, k):
                return tile[:, slot, k + 2].rearrange("q m s -> q (m s)")

            pe.wait_ge(ones_ready, 1)
            pe.wait_ge(band_lo_ready, 1)
            for j, tile in enumerate((band_hi, band_lo)):
                for i, k in enumerate(PAIRS):
                    o, r = columns(k, 2)
                    last = nc.tensor.matmul(ps_y[0][:, o], bands(tile, 0, k), ones[:, r],
                                            start=(i + j == 0), stop=(i == 4 and j == 1))
            last.then_inc(norm_done, 1)

            def blur_channel(base, k):
                pe.wait_ge(band_lo_ready, base + k + 1)
                pe.wait_ge(x_lo_ready, base + k + 1)
                if not (isinstance(base, int) and base + k < R):
                    pe.wait_ge(blur_ready, base + k - R + 1)
                slot = k % R
                parts = ((band_hi, x_hi), (band_hi, x_lo), (band_lo, x_hi))
                for j, (b, v) in enumerate(parts):
                    for i, off in enumerate(PAIRS):
                        o, r = columns(off, B)
                        last = nc.tensor.matmul(ps_blur[slot][:, o], bands(b, slot, off), v[:, slot, r],
                                                start=(i + j == 0), stop=(i == 4 and j == 2))
                last.then_inc(blur_done, 1)

            for k in range(R):
                blur_channel(0, k)
            with pe.Fori(R, C - R + 1, R) as c0:
                for k in range(R):
                    blur_channel(c0, k)

            pe.wait_ge(inv_ready, 1)
            pe.wait_ge(sign_band_ready, RP)
            pe.wait_ge(taps_loaded, 16 * C)

            def binary_conv(n, half, reused):
                plan = {0: ((1, 1, 0), (2, 0, 0), (0, 0, -1)), 1: ((1, 0, 0), (0, 1, 0), (2, 1, 1))}
                for q in range(2):
                    if reused:
                        pe.wait_ge((even_ready, odd_ready)[q], n - 1)
                    for i, (dx, place, off) in enumerate(plan[q]):
                        o, r = columns(off, B)
                        last = nc.tensor.matmul(
                            ps_y[2 * half + q][:, o],
                            sign_band[:, dx].rearrange("q r m -> q (r m)"),
                            taps[:, bass.ds(n, 1), place, r].rearrange("q a n -> q (a n)"),
                            start=(i == 0), stop=(i == 2))
                    last.then_inc(y_done, 1)

            binary_conv(0, 0, False)
            binary_conv(1, 1, False)
            binary_conv(2, 0, True)
            with pe.Fori(3, BLOCKS - 1, 2) as n:
                binary_conv(n, 1, True)
                binary_conv(n + 1, 0, True)


_INS = ["x", "L0_conv_filt", "L1_conv_weights"]


def kernel(**inputs):
    import numpy as _np
    import concourse.bacc as _bacc
    from concourse import mybir as _mybir
    from concourse.bass_utils import run_bass_kernel_spmd as _run

    nc = _bacc.Bacc("TRN2", target_bir_lowering=False, num_devices=1)
    arrays, args = {}, []
    for name in _INS:
        a = _np.ascontiguousarray(inputs[name])
        arrays[f"in_{name}_dram"] = a
        args.append(nc.dram_tensor(f"in_{name}_dram", a.shape, _mybir.dt.from_np(a.dtype), kind="ExternalInput").ap())
    dt = _mybir.dt.from_np(_np.dtype("float32"))
    args.append(nc.dram_tensor("out_0_dram", inputs["x"].shape, dt, kind="ExternalOutput").ap())
    blur_binary_conv(nc, *args)
    r = _run(nc, [arrays], core_ids=[0])
    return r.results[0]["out_0_dram"]
```

```python
import concourse.bass as bass
from concourse import mybir
from contextlib import ExitStack


def blur_binary_conv(nc, x, filt, weights, out):
    f32, f32r, bf16 = mybir.dt.float32, mybir.dt.float32r, mybir.dt.bfloat16
    ALU, ACT, AX = mybir.AluOpType, mybir.ActivationFunctionType, mybir.AxisListType

    B, C, H, W = x.shape
    K1 = filt.shape[2]
    K2 = 3
    CO = out.shape[1]
    WP = W // 2
    G = 2
    GB = B // G
    NG = WP * GB
    N = G * NG
    PAIR = 2
    PAIRS = [0, -2, -1, 1, 2]
    SLOTS = K1 + 1
    TAP0 = H - 1 - K1 // 2
    PITCH = TAP0 + K1

    KR, OR = 8, 6
    BLOCKS = -(-H // OR)
    LAST = H - OR * (BLOCKS - 1)
    RP = 2
    HALF = 64
    USED = OR // RP * CO
    TOP, BOTTOM = 3, 1
    ROWS = TOP + H + BOTTOM
    VLEN = K2 * CO * KR + KR

    R = 4
    FULL = C - R
    WARM_UP = 22
    AHEAD = 8
    SPLIT = 4

    filt_pad = nc.dram_tensor("filt_pad", (PITCH * (C * SLOTS + 2),), f32)
    sign_pad = nc.dram_tensor("sign_pad", (C, VLEN), bf16)
    act = nc.dram_tensor("act_signs", (C, G, ROWS, 2, NG), bf16)

    ctx = ExitStack()
    with ctx:
        def sb(name, shape, dt):
            return ctx.enter_context(nc.sbuf_tensor(name, shape, dt))

        def sem(name):
            return ctx.enter_context(nc.semaphore(name))

        filt_sb = sb("filt_sb", [C, K1 * K1], f32)
        filt_rows = sb("filt_rows", [C, SLOTS * PITCH], f32)
        w_in = sb("w_in", [C, CO, K2 * K2], f32)
        w_out = sb("w_out", [128, C * K2 * K2], f32)
        w_abs = sb("w_abs", [128, C * K2 * K2], f32)
        w_sum = sb("w_sum", [128, 1], f32)
        scale = sb("scale", [128, 1], f32)
        sign_rows = sb("sign_rows", [C, VLEN], bf16)
        zeros = sb("zeros", [C * G, TOP * NG], f32)
        idle = sb("idle", [128, N], bf16)
        ones = sb("ones", [128, 2 * WP], f32r)
        inv_pairs = sb("inv_pairs", [128, WP, 2], f32)
        inv_norm = sb("inv_norm", [128, WP, GB], f32)
        x_raw = sb("x_raw", [128, R // PAIR, B, W], f32)
        x_pair = sb("x_pair", [128, R, G, WP, GB], f32)
        x_hi = sb("x_hi", [128, R, G, NG], f32r)
        x_lo = sb("x_lo", [128, R, G, NG], f32r)
        band = sb("band", [128, R, SLOTS, PITCH], f32)
        band_hi = sb("band_hi", [128, R, SLOTS // 2, H, 2], f32r)
        band_lo = sb("band_lo", [128, R, SLOTS // 2, H, 2], f32r)
        blur = sb("blur", [128, R, G, NG], f32)
        signs = sb("signs", [128, R, G, NG], bf16)
        taps = sb("taps", [128, G, BLOCKS, 2, NG], bf16)
        sign_band_in = sb("sign_band_in", [128, K2, CO, KR], bf16)
        sign_band = sb("sign_band", [128, K2, RP, HALF], bf16)
        y_sb = sb("y_sb", [128, (BLOCKS + 1) // 2, B, RP, W], f32)

        ps_a = [ctx.enter_context(nc.psum_tensor(f"ps_a{i}", [128, N], f32)) for i in range(R)]
        ps_b = [ctx.enter_context(nc.psum_tensor(f"ps_b{i}", [128, N], f32)) for i in range(R)]

        filt_loaded, w_loaded = sem("filt_loaded"), sem("w_loaded")
        rows_zeroed, signs_zeroed, zeros_ready, ones_ready = (
            sem("rows_zeroed"), sem("signs_zeroed"), sem("zeros_ready"), sem("ones_ready"))
        idle_zeroed = sem("idle_zeroed")
        filt_placed, filt_padded = sem("filt_placed"), sem("filt_padded")
        sign_placed, sign_padded, sign_band_loaded = (
            sem("sign_placed"), sem("sign_padded"), sem("sign_band_loaded"))
        sign_band_zeroed, sign_band_ready = sem("sign_band_zeroed"), sem("sign_band_ready")
        bottom_padded = sem("bottom_padded")
        x_single = [sem(f"x_single{k}") for k in range(R)]
        band_single = [sem(f"band_single{k}") for k in range(R)]
        x_loaded = [sem(f"x_loaded{i}") for i in range(R // PAIR)]
        band_loaded = [sem(f"band_loaded{i}") for i in range(R // PAIR)]
        x_paired, x_hi_ready, x_lo_ready = sem("x_paired"), sem("x_hi_ready"), sem("x_lo_ready")
        band_hi_ready, band_lo_ready = sem("band_hi_ready"), sem("band_lo_ready")
        pairs_ready, inv_ready = sem("pairs_ready"), sem("inv_ready")
        products_done = sem("products_done")
        blur_ready, signs_ready = sem("blur_ready"), sem("signs_ready")
        signs_stored = [sem(f"signs_stored{i}") for i in range(R)]
        half_done, half_ready, half_signs = sem("half_done"), sem("half_ready"), sem("half_signs")
        half_stored = [[sem(f"half_stored{g}_{k}") for k in range(R)] for g in range(G)]
        taps_loaded = [sem(f"taps_loaded{g}") for g in range(G)]
        last_taps_loaded = [sem(f"last_taps_loaded{g}") for g in range(G)]
        abs_ready, sum_ready, scale_ready = sem("abs_ready"), sem("sum_ready"), sem("scale_ready")
        y_done = sem("y_done")
        upper_ready, lower_ready = sem("upper_ready"), sem("lower_ready")
        sp_stored, pool_stored = sem("sp_stored"), sem("pool_stored")

        block = ctx.enter_context(nc.Block())

        def pair_slot(k):
            return k // PAIR % (R // PAIR)

        def landed(base, k, per_round):
            return base * (per_round // R) + per_round * (k // R + 1)

        def wait_loaded(eng, single, by_pair, per_load, base, k):
            if isinstance(base, int) and not R <= base + k < C - PAIR:
                eng.wait_ge(single[k % R], per_load * (1 if base + k < R else 2))
            else:
                eng.wait_ge(by_pair[pair_slot(k)], landed(base - R, k, per_load))

        def slots(k):
            return band[:, k % R, :, 0:H].rearrange("q (o s) m -> q o s m", s=2)

        def by_slot(tile, k):
            return tile[:, k % R].rearrange("q o m s -> q o s m")

        HALF_BLOCKS = ([(n, g) for g in range(G) for n in range(AHEAD)]
                       + [(n, g) for n in range(AHEAD, BLOCKS) for g in range(G)])

        def load_taps(eng, c, g, loaded):
            eng.dma_start(taps[c * KR:(c + 1) * KR, g].rearrange("r b p n -> r b (p n)"),
                          bass.AP(act, (c * G + g) * ROWS * 2 * NG,
                                  [[2 * NG, KR], [OR * 2 * NG, BLOCKS], [1, 2 * NG]])
                          ).then_inc(loaded, 16)

        def load_full_taps(eng, g):
            eng.wait_ge(bottom_padded, 16)
            for c in range(FULL):
                eng.wait_ge(signs_stored[c % R], 16 + landed(0, c, 16))
                load_taps(eng, c, g, taps_loaded[g])

        def store_rows(eng, n, pair, images, stored):
            q = n % 2 * HALF + pair * CO
            row = OR * (BLOCKS - 1 - n) + RP * pair
            eng.dma_start(out[images, :, row:row + RP].rearrange("i c r w -> c i (r w)"),
                          y_sb[q:q + CO, n // 2, images].rearrange("q i r w -> q i (r w)")
                          ).then_inc(stored, 16)

        def store_output(eng, share, stored):
            parts = [(n, 0, slice(0, GB)) for n in range(SPLIT)]
            parts += [(n, G - 1, slice(GB, B) if n < SPLIT else slice(0, B)) for n in range(BLOCKS)]
            stores = 0
            for n, g, images in parts:
                if share(n):
                    eng.wait_ge(upper_ready, HALF_BLOCKS.index((n, g)) + 1)
                    eng.wait_ge(lower_ready, HALF_BLOCKS.index((n, g)) + 1)
                for pair in share(n):
                    store_rows(eng, n, pair, images, stored)
                stores += len(share(n))
            eng.wait_ge(stored, 16 * stores)

        def pool_share(n):
            return [(OR if n else LAST) // RP - 1] if n < BLOCKS - 1 else []

        def sp_share(n):
            return [pair for pair in range((OR if n else LAST) // RP) if pair not in pool_share(n)]

        def pad_signs(eng):
            rows = act[:].rearrange("c g r p n -> (c g) r (p n)")
            for k in range(R):
                q = slice(k * C * G // R, (k + 1) * C * G // R)
                eng.dma_start(rows[q, 0:TOP].rearrange("q r n -> q (r n)"),
                              zeros[q, :].bitcast(bf16)).then_inc(signs_stored[k], 16)
            eng.dma_start(rows[:, TOP + H], zeros[:, 0:NG].bitcast(bf16)).then_inc(bottom_padded, 16)

        @block.gpsimd
        def _(pool):
            nc.gpsimd.memset(filt_rows[:, :], 0.0).then_inc(rows_zeroed, 1)
            nc.gpsimd.memset(zeros[:, :], 0.0).then_inc(zeros_ready, 1)
            nc.gpsimd.memset(ones[:, :].bitcast(f32), 1.0).then_inc(ones_ready, 1)
            nc.gpsimd.memset(sign_rows[:, :], 0.0).then_inc(signs_zeroed, 1)
            nc.gpsimd.memset(sign_band[:, :, :, :], 0.0).then_inc(sign_band_zeroed, 1)
            pool.dma_start(w_in[:, :, :],
                           bass.AP(weights.tensor, 0, [[K2 * K2, C], [C * K2 * K2, CO], [1, K2 * K2]])
                           ).then_inc(w_loaded, 16)
            pool.dma_start(w_out[:, :],
                           bass.AP(weights.tensor, 0, [[0, 128 // CO], [C * K2 * K2, CO], [1, C * K2 * K2]])
                           ).then_inc(w_loaded, 16)
            pool.wait_ge(sign_placed, K2)
            pool.dma_start(sign_pad[:, :], sign_rows[:, :]).then_inc(sign_padded, 16)
            pool.wait_ge(sign_padded, 16)
            for kr in range(KR):
                pool.dma_start(sign_band_in[kr::KR].rearrange("c d o m -> c (d o m)"),
                               sign_pad[:, kr:kr + K2 * CO * KR]).then_inc(sign_band_loaded, 16)
            pool.wait_ge(band_lo_ready, C - R)
            load_full_taps(pool, 1)
            store_output(pool, pool_share, pool_stored)

        @block.sync
        def _(sp):
            def load_x(channels, loaded):
                c, k = channels.start, channels.start % PAIR
                n = channels.stop - c
                sp.dma_start(x_raw[k * H:(k + n) * H, pair_slot(c)],
                             x[:, channels].rearrange("i c h w -> (c h) i w")).then_inc(loaded, 16)

            def load_band(channels, loaded):
                c, n = channels.start, channels.stop - channels.start
                for p in range(2):
                    sp.dma_start(band[p * H:(p + 1) * H, c % R:c % R + n].rearrange("r c s m -> r (c s m)"),
                                 bass.AP(filt_pad, (c * SLOTS + p) * PITCH,
                                         [[1, H], [1, n * SLOTS * PITCH]])).then_inc(loaded, 16)

            sp.dma_start(filt_sb[:, :], filt.rearrange("c a h w -> c (a h w)")).then_inc(filt_loaded, 16)
            load_x(slice(0, 1), x_single[0])
            sp.wait_ge(zeros_ready, 1)
            sp.dma_start(bass.AP(filt_pad, C * SLOTS * PITCH, [[1, 1], [1, 2 * PITCH]]),
                         zeros[0:1, 0:2 * PITCH]).then_inc(filt_padded, 16)
            sp.wait_ge(filt_placed, 1)
            sp.dma_start(bass.AP(filt_pad, 0, [[SLOTS * PITCH, C], [1, SLOTS * PITCH]]),
                         filt_rows[:, :]).then_inc(filt_padded, 16)
            load_x(slice(1, 2), x_single[1])
            sp.wait_ge(filt_padded, 32)
            for k in range(R):
                if k > 1:
                    load_x(slice(k, k + 1), x_single[k])
                load_band(slice(k, k + 1), band_single[k])
            pad_signs(sp)
            for c in range(R, C - PAIR, PAIR):
                sp.wait_ge(x_paired, c + PAIR - R)
                load_x(slice(c, c + PAIR), x_loaded[pair_slot(c)])
                sp.wait_ge(band_lo_ready, c + PAIR - R)
                load_band(slice(c, c + PAIR), band_loaded[pair_slot(c)])
            for c in range(C - PAIR, C):
                sp.wait_ge(x_paired, c + 1 - R)
                load_x(slice(c, c + 1), x_single[c % R])
                sp.wait_ge(band_lo_ready, c + 1 - R)
                load_band(slice(c, c + 1), band_single[c % R])
            load_full_taps(sp, 0)
            for g in range(G):
                for k in range(R):
                    sp.wait_ge(half_stored[g][k], 16)
                    load_taps(sp, FULL + k, g, last_taps_loaded[g])
            store_output(sp, sp_share, sp_stored)

        @block.vector
        def _(dve):
            nc.vector.memset(idle[:, :].bitcast(f32), 0.0).then_inc(idle_zeroed, 1)
            dve.wait_ge(rows_zeroed, 1)
            dve.wait_ge(filt_loaded, 16)
            nc.vector.tensor_copy(
                filt_rows[:, :].rearrange("c (s m) -> c s m", m=PITCH)[:, 1:1 + K1, TAP0:TAP0 + K1],
                filt_sb[:, :].rearrange("c (y x) -> c x y", x=K1)).then_inc(filt_placed, 1)

            def pair_columns(base, k):
                wait_loaded(dve, x_single, x_loaded, 16, base, k)
                u = k % PAIR
                for p in range(2):
                    last = nc.vector.tensor_copy(
                        x_pair[p * H:(p + 1) * H, k % R].rearrange("h g j i -> h g i j"),
                        x_raw[u * H:(u + 1) * H, pair_slot(k), :, p::2].rearrange(
                            "h (g i) j -> h g i j", g=G))
                last.then_inc(x_paired, 1)

            def low_parts(base, k):
                dve.wait_ge(x_hi_ready, base + k + 1)
                if not (isinstance(base, int) and base + k < R - 1):
                    dve.wait_ge(products_done, base + k - R + 2)
                nc.vector.tensor_tensor(x_lo[:, k % R].rearrange("q g n -> q (g n)"),
                                        x_pair[:, k % R].rearrange("q g j i -> q (g j i)"),
                                        x_hi[:, k % R].rearrange("q g n -> q (g n)").bitcast(f32),
                                        ALU.subtract).then_inc(x_lo_ready, 1)
                dve.wait_ge(band_hi_ready, base + k + 1)
                nc.vector.tensor_tensor(by_slot(band_lo, k), slots(k), by_slot(band_hi, k).bitcast(f32),
                                        ALU.subtract).then_inc(band_lo_ready, 1)

            def inverse_norm():
                dve.wait_ge(products_done, 2)
                nc.vector.reciprocal(inv_pairs[:, :, :],
                                     ps_b[0][:, 0:2 * WP].rearrange("q (j i) -> q j i", i=2)
                                     ).then_inc(pairs_ready, 1)
                dve.wait_ge(pairs_ready, 1)
                nc.vector.tensor_copy(inv_norm[:, :, :], inv_pairs[:, :, 0:1].to_broadcast([128, WP, GB])
                                      ).then_inc(inv_ready, 1)
                dve.wait_ge(inv_ready, 1)

            both_halves = bass.AP(inv_norm, 0, [[NG, 128], [0, G], [1, NG]])

            def normalise(base, k):
                dve.wait_ge(products_done, base + k + 2)
                nc.vector.tensor_tensor(blur[:, k % R],
                                        ps_a[k % R][:, :].rearrange("q (g n) -> q g n", g=G),
                                        both_halves, ALU.mult).then_inc(blur_ready, 1)

            def normalise_half(g, k):
                dve.wait_ge(half_done, g * R + k + 1)
                if g == 0:
                    dve.wait_ge(signs_ready, FULL - R + k + 1)
                nc.vector.tensor_tensor(blur[:, k, g], (ps_a, ps_b)[g][k][:, 0:NG],
                                        inv_norm[:, :, :].rearrange("q j i -> q (j i)"), ALU.mult
                                        ).then_inc(half_ready, 1)

            def weight_scales():
                dve.wait_ge(w_loaded, 32)
                nc.vector.scalar_tensor_tensor(out=w_abs[:, :], in0=w_out[:, :], scalar=-1.0,
                                               in1=w_out[:, :], op0=ALU.mult, op1=ALU.max
                                               ).then_inc(abs_ready, 1)
                dve.wait_ge(abs_ready, 1)
                nc.vector.reduce_sum(w_sum[:, :], w_abs[:, :], axis=AX.X).then_inc(sum_ready, 1)
                dve.wait_ge(sum_ready, 1)
                nc.vector.tensor_scalar(scale[:, :], w_sum[:, :], 1.0 / (C * K2 * K2), None, ALU.mult
                                        ).then_inc(scale_ready, 1)

            def sign_matrices():
                dve.wait_ge(sign_band_zeroed, 1)
                dve.wait_ge(sign_band_loaded, 16 * KR)
                for rp in range(RP):
                    nc.vector.tensor_copy(
                        sign_band[:, :, rp, 0:USED].rearrange("q d (m o) -> q d o m", o=CO),
                        sign_band_in[:, :, :, rp:OR:RP]).then_inc(sign_band_ready, 1)

            for k in range(R - 1):
                pair_columns(0, k)
                low_parts(0, k)
            pair_columns(0, R - 1)
            inverse_norm()
            normalise(0, 0)
            low_parts(0, R - 1)
            pair_columns(R, 0)
            normalise(0, 1)
            with dve.Fori(R, FULL - R + 1, R) as c0:
                for k in range(R):
                    pair_columns(c0, k + 1)
                    low_parts(c0, k)
                    normalise(c0, k - 2)
            for k in range(R):
                if k < R - 1:
                    pair_columns(FULL, k + 1)
                low_parts(FULL, k)
                if k < 2:
                    normalise(FULL, k - 2)
            for k in range(R):
                normalise_half(0, k)
            weight_scales()
            sign_matrices()
            for k in range(R):
                normalise_half(1, k)

            def scale_lower(s, n2, odd, g, k):
                dve.wait_ge(y_done, s + 1)
                nc.vector.tensor_scalar(
                    y_sb[odd * HALF:odd * HALF + USED, bass.ds(n2, 1), g * GB:(g + 1) * GB, 1].rearrange(
                        "q a i (j e) -> q e j (a i)", e=2),
                    ps_a[k][HALF:HALF + USED, :].rearrange("q (e j i) -> q e j i", e=2, i=GB),
                    scale[HALF:HALF + USED, 0:1], None, ALU.mult).then_inc(lower_ready, 1)

            for g in range(G):
                with dve.Fori(0, AHEAD // R, 1) as a:
                    for k in range(R):
                        scale_lower(g * AHEAD + R * a + k, 2 * a + k // 2, k % 2, g, k)
            for s in range(G * AHEAD, G * BLOCKS):
                n, g = HALF_BLOCKS[s]
                scale_lower(s, n // 2, n % 2, g, s % R)

        @block.scalar
        def _(act_e):
            def high_parts(base, k):
                if not (isinstance(base, int) and base + k < R):
                    act_e.wait_ge(products_done, base + k - R + 2)
                act_e.wait_ge(x_paired, base + k + 1)
                nc.scalar.activation(x_hi[:, k % R].rearrange("q g n -> q (g n)"),
                                     x_pair[:, k % R].rearrange("q g j i -> q (g j i)"),
                                     ACT.Copy).then_inc(x_hi_ready, 1)
                wait_loaded(act_e, band_single, band_loaded, 32, base, k)
                nc.scalar.activation(by_slot(band_hi, k), slots(k), ACT.Copy).then_inc(band_hi_ready, 1)

            def take_signs(base, k):
                act_e.wait_ge(blur_ready, base + k + 1)
                act_e.wait_ge(signs_stored[k % R], landed(base, k, 16))
                nc.scalar.activation(signs[:, k % R], blur[:, k % R], ACT.Sign).then_inc(signs_ready, 1)
                act_e.wait_ge(signs_ready, base + k + 1)
                act_e.dma_start(
                    act[bass.ds(base + k, 1), :, TOP:TOP + H].rearrange("c g m p n -> (c m p) g n"),
                    signs[:, k % R]).then_inc(signs_stored[k % R], 16)

            def take_signs_half(g, k):
                act_e.wait_ge(half_ready, g * R + k + 1)
                if g == 0:
                    act_e.wait_ge(signs_stored[k], landed(0, FULL + k, 16))
                nc.scalar.activation(signs[:, k, g], blur[:, k, g], ACT.Sign).then_inc(half_signs, 1)
                act_e.wait_ge(half_signs, g * R + k + 1)
                act_e.dma_start(act[FULL + k, g, TOP:TOP + H].rearrange("m p n -> (m p) n"),
                                signs[:, k, g]).then_inc(half_stored[g][k], 16)

            def place_signs():
                act_e.wait_ge(w_loaded, 32)
                act_e.wait_ge(signs_zeroed, 1)
                rows = sign_rows[:, 0:K2 * CO * KR].rearrange("c (d o m) -> c d o m", o=CO, m=KR)
                for dy in range(K2):
                    nc.scalar.activation(
                        rows[:, :, :, KR - 1 - dy],
                        w_in[:, :, dy * K2:(dy + 1) * K2].rearrange("c o d -> c d o"),
                        ACT.Sign).then_inc(sign_placed, 1)

            for k in range(R):
                high_parts(0, k)
            place_signs()
            take_signs(0, 0)
            with act_e.Fori(R, FULL - R + 1, R) as c0:
                for k in range(R):
                    high_parts(c0, k)
                    take_signs(c0, k - 3)
            for k in range(R):
                high_parts(FULL, k)
                if k < 3:
                    take_signs(FULL, k - 3)
            for g in range(G):
                for k in range(R):
                    take_signs_half(g, k)

            def scale_upper(s, n2, odd, g, k):
                act_e.wait_ge(y_done, s + 1)
                nc.scalar.activation(
                    y_sb[odd * HALF:odd * HALF + USED, bass.ds(n2, 1), g * GB:(g + 1) * GB, 0].rearrange(
                        "q a i (j e) -> q e j (a i)", e=2),
                    ps_a[k][0:USED, :].rearrange("q (e j i) -> q e j i", e=2, i=GB),
                    ACT.Copy, scale=scale[0:USED, 0:1]).then_inc(upper_ready, 1)

            act_e.wait_ge(scale_ready, 1)
            for g in range(G):
                with act_e.Fori(0, AHEAD // R, 1) as a:
                    for k in range(R):
                        scale_upper(g * AHEAD + R * a + k, 2 * a + k // 2, k % 2, g, k)
            for s in range(G * AHEAD, G * BLOCKS):
                n, g = HALF_BLOCKS[s]
                scale_upper(s, n // 2, n % 2, g, s % R)

        @block.tensor
        def _(pe):
            def columns(k, per):
                lo, hi = max(0, -k), WP - max(0, k)
                return slice(lo * per, hi * per), slice((lo + k) * per, (hi + k) * per)

            def bands(tile, slot, k):
                return tile[:, slot, k + 2].rearrange("q m s -> q (m s)")

            PARTS = ((band_hi, x_hi), (band_hi, x_lo), (band_lo, x_hi))

            def warm_up():
                pe.wait_ge(idle_zeroed, 1)
                for _ in range(WARM_UP):
                    nc.tensor.matmul(ps_b[R - 1][:, :], idle[:, 0:128], idle[:, :], start=True, stop=True)

            def norm():
                pe.wait_ge(ones_ready, 1)
                for j, tile in enumerate((band_hi, band_lo)):
                    for i, off in enumerate(PAIRS):
                        o, r = columns(off, 2)
                        last = nc.tensor.matmul(ps_b[0][:, o], bands(tile, 0, off), ones[:, r],
                                                start=(i + j == 0), stop=(i == 4 and j == 1))
                last.then_inc(products_done, 1)

            def blur_channel(base, k):
                pe.wait_ge(x_lo_ready, base + k + 1)
                if isinstance(base, int) and base + k == 0:
                    pe.wait_ge(band_hi_ready, 1)
                else:
                    pe.wait_ge(band_lo_ready, base + k + 1)
                if not (isinstance(base, int) and base + k < R):
                    pe.wait_ge(blur_ready, base + k - R + 1)
                slot = k % R
                bank = ps_a[slot][:, :].rearrange("q (g n) -> q g n", g=G)
                for j, (b, v) in enumerate(PARTS):
                    if isinstance(base, int) and base + k + 2 == j:
                        pe.wait_ge(band_lo_ready, 1)
                    for i, off in enumerate(PAIRS):
                        o, r = columns(off, GB)
                        last = nc.tensor.matmul(bank[:, :, o], bands(b, slot, off), v[:, slot, :, r],
                                                start=(i + j == 0), stop=(i == 4 and j == 2))
                last.then_inc(products_done, 1)

            def blur_half(g, k):
                if g == 0:
                    pe.wait_ge(band_lo_ready, FULL + k + 1)
                    pe.wait_ge(x_lo_ready, FULL + k + 1)
                    pe.wait_ge(blur_ready, FULL + k - R + 1)
                for j, (b, v) in enumerate(PARTS):
                    for i, off in enumerate(PAIRS):
                        o, r = columns(off, GB)
                        last = nc.tensor.matmul((ps_a, ps_b)[g][k][:, o], bands(b, k, off), v[:, k, g, r],
                                                start=(i + j == 0), stop=(i == 4 and j == 2))
                last.then_inc(half_done, 1)

            warm_up()
            blur_channel(0, 0)
            norm()
            for k in range(1, R):
                blur_channel(0, k)
            with pe.Fori(R, FULL - R + 1, R) as c0:
                for k in range(R):
                    blur_channel(c0, k)
            pe.wait_ge(inv_ready, 1)
            for g in range(G):
                for k in range(R):
                    blur_half(g, k)

            PLAN = {0: ((1, 1, 0), (2, 0, 0), (0, 0, -1)), 1: ((1, 0, 0), (0, 1, 0), (2, 1, 1))}

            def half_block(s, n, g, k):
                if not (isinstance(s, int) and s < R):
                    pe.wait_ge(upper_ready, s - R + 1)
                    pe.wait_ge(lower_ready, s - R + 1)
                for q in range(2):
                    bank = ps_a[k][:, q * NG:(q + 1) * NG]
                    for i, (dx, place, off) in enumerate(PLAN[q]):
                        o, r = columns(off, GB)
                        last = nc.tensor.matmul(
                            bank[:, o], sign_band[:, dx].rearrange("q r m -> q (r m)"),
                            taps[:, g, bass.ds(n, 1), place, r].rearrange("q a n -> q (a n)"),
                            start=(i == 0), stop=(i == 2))
                last.then_inc(y_done, 1)

            pe.wait_ge(sign_band_ready, RP)
            pe.wait_ge(half_ready, R)
            pe.wait_ge(taps_loaded[0], 16 * FULL)
            pe.wait_ge(last_taps_loaded[0], 16 * R)
            for n in range(AHEAD):
                half_block(n, n, 0, n % R)
            pe.wait_ge(taps_loaded[1], 16 * FULL)
            pe.wait_ge(last_taps_loaded[1], 16 * R)
            with pe.Fori(0, AHEAD // R, 1) as a:
                for k in range(R):
                    half_block(AHEAD + R * a + k, R * a + k, 1, k)
            for s in range(G * AHEAD, G * BLOCKS):
                n, g = HALF_BLOCKS[s]
                half_block(s, n, g, s % R)


_INS = ["x", "L0_conv_filt", "L1_conv_weights"]


def kernel(**inputs):
    import numpy as _np
    import concourse.bacc as _bacc
    from concourse import mybir as _mybir
    from concourse.bass_utils import run_bass_kernel_spmd as _run

    nc = _bacc.Bacc("TRN2", target_bir_lowering=False, num_devices=1)
    arrays, args = {}, []
    for name in _INS:
        a = _np.ascontiguousarray(inputs[name])
        arrays[f"in_{name}_dram"] = a
        args.append(nc.dram_tensor(f"in_{name}_dram", a.shape, _mybir.dt.from_np(a.dtype), kind="ExternalInput").ap())
    dt = _mybir.dt.from_np(_np.dtype("float32"))
    args.append(nc.dram_tensor("out_0_dram", inputs["x"].shape, dt, kind="ExternalOutput").ap())
    blur_binary_conv(nc, *args)
    r = _run(nc, [arrays], core_ids=[0])
    return r.results[0]["out_0_dram"]
```
